# Optimizing a Trainium2 kernel written in Bass

```python
import numpy as np
import jax
import jax.numpy as jnp

def _softmax(x, axis=-1):
    return jax.nn.softmax(x, axis=axis)

def _gelu(x):
    return jax.nn.gelu(x, approximate=True)

def _silu(x):
    return jax.nn.silu(x)

def _sigmoid(x):
    return jax.nn.sigmoid(x)

def _layernorm(x, axis=-1, eps=1e-05):
    m = jnp.mean(x, axis=axis, keepdims=True)
    v = jnp.var(x, axis=axis, keepdims=True)
    return (x - m) / jnp.sqrt(v + eps)

def _scatter_add(tgt, idx, src, axis=0):
    return tgt.at[idx].add(src)

def _segment_sum(src, seg, n):
    return jax.ops.segment_sum(src, seg, n)
kernel_name = 'mk_prb_d1_jaxref_r8_b8a66d'

def setup_inputs(seed: int=0):
    np.random.seed(seed)
    _w = jnp.asarray

    def _L0_attn_setup():
        import jax, jax.numpy as jnp
        import numpy as np
        D_MODEL = 256
        NUM_HEADS = 16
        D_KV = D_MODEL // NUM_HEADS
        THETA = 10000.0
        N_LORA = 4
        RANK = 16
        BATCH = 2
        SEQ = 256

        def _adapter_ids(starts, batch):
            ids = jnp.searchsorted(starts, jnp.arange(batch), side='right') - 1
            return jnp.clip(ids, 0, starts.shape[0] - 1)

        def _multilora(x, ids, W, A, B):
            base = jnp.einsum('bsd,od->bso', x, W)
            Ai, Bi = (A[ids], B[ids])
            low = jnp.einsum('bsd,brd->bsr', x, Ai)
            return base + jnp.einsum('bsr,bor->bso', low, Bi)

        def _rope(x):
            d = x.shape[-1]
            pos = jnp.arange(x.shape[-2], dtype=jnp.float32)
            inv_freq = THETA ** (-jnp.arange(0, d, 2, dtype=jnp.float32) / d)
            ang = pos[:, None] * inv_freq[None, :]
            cos, sin = (jnp.cos(ang), jnp.sin(ang))
            x1, x2 = (x[..., 0::2], x[..., 1::2])
            o1 = x1 * cos - x2 * sin
            o2 = x1 * sin + x2 * cos
            return jnp.stack([o1, o2], axis=-1).reshape(x.shape)
        key = jax.random.key(seed)
        ks = jax.random.split(key, 16)
        s = 0.02
        inp = {'x': jax.random.normal(ks[0], (BATCH, SEQ, D_MODEL), jnp.float32), 'lora_start_indices': jnp.sort(jax.random.randint(ks[1], (N_LORA,), 0, BATCH)), 'Wq': jax.random.normal(ks[2], (D_MODEL, D_MODEL), jnp.float32) * s, 'Aq': jax.random.normal(ks[3], (N_LORA, RANK, D_MODEL), jnp.float32) * s, 'Bq': jax.random.normal(ks[4], (N_LORA, D_MODEL, RANK), jnp.float32) * s, 'Wk': jax.random.normal(ks[5], (D_MODEL, D_MODEL), jnp.float32) * s, 'Ak': jax.random.normal(ks[6], (N_LORA, RANK, D_MODEL), jnp.float32) * s, 'Bk': jax.random.normal(ks[7], (N_LORA, D_MODEL, RANK), jnp.float32) * s, 'Wv': jax.random.normal(ks[8], (D_MODEL, D_MODEL), jnp.float32) * s, 'Av': jax.random.normal(ks[9], (N_LORA, RANK, D_MODEL), jnp.float32) * s, 'Bv': jax.random.normal(ks[10], (N_LORA, D_MODEL, RANK), jnp.float32) * s, 'Wo': jax.random.normal(ks[11], (D_MODEL, D_MODEL), jnp.float32) * s, 'Ao': jax.random.normal(ks[12], (N_LORA, RANK, D_MODEL), jnp.float32) * s, 'Bo': jax.random.normal(ks[13], (N_LORA, D_MODEL, RANK), jnp.float32) * s}
        return inp
    _L0_attn_in = _L0_attn_setup()

    def _L0_ffn_setup():
        import jax, jax.numpy as jnp
        import numpy as np
        HIDDEN = 256
        INTER = 96
        N_EXPERTS = 64
        TOP_K = 8
        key = jax.random.key(seed)
        k0, k1, k2, k3, k4 = jax.random.split(key, 5)
        s = 0.02
        return {'hidden_states': jax.random.normal(k0, (1, 128, HIDDEN), dtype=jnp.float32), 'gate_w': jax.random.normal(k1, (N_EXPERTS, HIDDEN), dtype=jnp.float32) * s, 'Wg': jax.random.normal(k2, (N_EXPERTS, INTER, HIDDEN), dtype=jnp.float32) * s, 'Wu': jax.random.normal(k3, (N_EXPERTS, INTER, HIDDEN), dtype=jnp.float32) * s, 'Wd': jax.random.normal(k4, (N_EXPERTS, HIDDEN, INTER), dtype=jnp.float32) * s}
    _L0_ffn_in = _L0_ffn_setup()
    _d = {'L0_attn_x': _L0_attn_in['x'], 'L0_attn_lora_start_indices': _L0_attn_in['lora_start_indices'], 'L0_attn_Wq': _L0_attn_in['Wq'], 'L0_attn_Aq': _L0_attn_in['Aq'], 'L0_attn_Bq': _L0_attn_in['Bq'], 'L0_attn_Wk': _L0_attn_in['Wk'], 'L0_attn_Ak': _L0_attn_in['Ak'], 'L0_attn_Bk': _L0_attn_in['Bk'], 'L0_attn_Wv': _L0_attn_in['Wv'], 'L0_attn_Av': _L0_attn_in['Av'], 'L0_attn_Bv': _L0_attn_in['Bv'], 'L0_attn_Wo': _L0_attn_in['Wo'], 'L0_attn_Ao': _L0_attn_in['Ao'], 'L0_attn_Bo': _L0_attn_in['Bo'], 'L0_ffn_gate_w': _L0_ffn_in['gate_w'], 'L0_ffn_Wg': _L0_ffn_in['Wg'], 'L0_ffn_Wu': _L0_ffn_in['Wu'], 'L0_ffn_Wd': _L0_ffn_in['Wd']}
    _x0 = _d['L0_attn_x']
    _d['L0_attn_x'] = jax.random.normal(jax.random.fold_in(jax.random.key(seed), 1), (2, 1024, 256), dtype=_x0.dtype)
    del _x0
    return _d

def reference(L0_attn_x, L0_attn_lora_start_indices, L0_attn_Wq, L0_attn_Aq, L0_attn_Bq, L0_attn_Wk, L0_attn_Ak, L0_attn_Bk, L0_attn_Wv, L0_attn_Av, L0_attn_Bv, L0_attn_Wo, L0_attn_Ao, L0_attn_Bo, L0_ffn_gate_w, L0_ffn_Wg, L0_ffn_Wu, L0_ffn_Wd):

    def _L0_attn_ref(x, lora_start_indices, Wq, Aq, Bq, Wk, Ak, Bk, Wv, Av, Bv, Wo, Ao, Bo):
        import jax, jax.numpy as jnp
        import numpy as np
        D_MODEL = 256
        NUM_HEADS = 16
        D_KV = D_MODEL // NUM_HEADS
        THETA = 10000.0
        N_LORA = 4
        RANK = 16
        BATCH = 2
        SEQ = 256

        def _adapter_ids(starts, batch):
            ids = jnp.searchsorted(starts, jnp.arange(batch), side='right') - 1
            return jnp.clip(ids, 0, starts.shape[0] - 1)

        def _multilora(x, ids, W, A, B):
            base = jnp.einsum('bsd,od->bso', x, W)
            Ai, Bi = (A[ids], B[ids])
            low = jnp.einsum('bsd,brd->bsr', x, Ai)
            return base + jnp.einsum('bsr,bor->bso', low, Bi)

        def _rope(x):
            d = x.shape[-1]
            pos = jnp.arange(x.shape[-2], dtype=jnp.float32)
            inv_freq = THETA ** (-jnp.arange(0, d, 2, dtype=jnp.float32) / d)
            ang = pos[:, None] * inv_freq[None, :]
            cos, sin = (jnp.cos(ang), jnp.sin(ang))
            x1, x2 = (x[..., 0::2], x[..., 1::2])
            o1 = x1 * cos - x2 * sin
            o2 = x1 * sin + x2 * cos
            return jnp.stack([o1, o2], axis=-1).reshape(x.shape)
        b, s, _ = x.shape
        ids = _adapter_ids(lora_start_indices, b)
        Q = _multilora(x, ids, Wq, Aq, Bq)
        K = _multilora(x, ids, Wk, Ak, Bk)
        V = _multilora(x, ids, Wv, Av, Bv)
        split = lambda t: t.reshape(b, s, NUM_HEADS, D_KV).transpose(0, 2, 1, 3)
        Q, K, V = (split(Q), split(K), split(V))
        Q, K = (_rope(Q), _rope(K))
        scores = jnp.einsum('bhqd,bhkd->bhqk', Q, K) / jnp.sqrt(jnp.asarray(D_KV, x.dtype))
        causal = jnp.tril(jnp.ones((s, s), bool))
        scores = jnp.where(causal, scores, jnp.asarray(-jnp.inf, scores.dtype))
        attn = jax.nn.softmax(scores, axis=-1)
        out = jnp.einsum('bhqk,bhkd->bhqd', attn, V)
        out = out.transpose(0, 2, 1, 3).reshape(b, s, D_MODEL)
        return _multilora(out, ids, Wo, Ao, Bo)

    def _L0_ffn_ref(hidden_states, gate_w, Wg, Wu, Wd):
        import jax, jax.numpy as jnp
        import numpy as np
        HIDDEN = 256
        INTER = 96
        N_EXPERTS = 64
        TOP_K = 8
        B, S, H = hidden_states.shape
        x = hidden_states.reshape(-1, H)
        T = x.shape[0]
        logits = jnp.einsum('th,eh->te', x, gate_w)
        probs = jax.nn.softmax(logits.astype(jnp.float32), axis=-1)
        top_w, top_i = jax.lax.top_k(probs, TOP_K)
        top_w = top_w / jnp.sum(top_w, axis=-1, keepdims=True)
        top_w = top_w.astype(x.dtype)
        w = jnp.zeros((T, N_EXPERTS), dtype=x.dtype)
        w = w.at[jnp.arange(T)[:, None], top_i].set(top_w)
        g = jnp.einsum('th,eih->eti', x, Wg)
        u = jnp.einsum('th,eih->eti', x, Wu)
        z = jax.nn.silu(g) * u * w.T[:, :, None]
        out = jnp.einsum('eti,ehi->th', z, Wd)
        return out.reshape(B, S, H)
    x = L0_attn_x
    xn = _layernorm(x, axis=-1)
    x = x + _L0_attn_ref(xn, L0_attn_lora_start_indices, L0_attn_Wq, L0_attn_Aq, L0_attn_Bq, L0_attn_Wk, L0_attn_Ak, L0_attn_Bk, L0_attn_Wv, L0_attn_Av, L0_attn_Bv, L0_attn_Wo, L0_attn_Ao, L0_attn_Bo) + _L0_ffn_ref(xn, L0_ffn_gate_w, L0_ffn_Wg, L0_ffn_Wu, L0_ffn_Wd)
    return x

_drawn_inputs = setup_inputs


def setup_inputs(seed=0):
    import zlib

    import numpy as np

    out = dict(_drawn_inputs(seed))
    spreads = {}
    factors = {'L0_attn_Wq': 8.0,
     'L0_attn_Aq': 8.0,
     'L0_attn_Bq': 8.0,
     'L0_attn_Wk': 8.0,
     'L0_attn_Ak': 8.0,
     'L0_attn_Bk': 8.0,
     'L0_attn_Wv': 6.378,
     'L0_attn_Av': 8.0,
     'L0_attn_Bv': 8.0,
     'L0_attn_Wo': 6.335,
     'L0_attn_Ao': 8.0,
     'L0_attn_Bo': 8.0,
     'L0_ffn_gate_w': 8.0,
     'L0_ffn_Wg': 8.0,
     'L0_ffn_Wu': 8.0,
     'L0_ffn_Wd': 8.0}
    for name, (base, spread) in spreads.items():
        noise = np.random.default_rng([zlib.crc32(name.encode()), seed]).standard_normal(out[name].shape)
        drawn = base * np.exp(spread * noise) if base else spread * noise
        out[name] = jnp.asarray(drawn.astype(out[name].dtype))
    for name, factor in factors.items():
        out[name] = (out[name] * factor).astype(out[name].dtype)
    return out
```

```python
from contextlib import ExitStack

import numpy as np
import concourse.bass as bass
from concourse import mybir

F32, BF16, I32 = mybir.dt.float32, mybir.dt.bfloat16, mybir.dt.int32
ALU, ACT, AX = mybir.AluOpType, mybir.ActivationFunctionType, mybir.AxisListType.X

P = 128
BATCH, SEQ, D = 2, 1024, 256
H, DK = 16, 16
N_LORA, RANK = 4, 16
E, TOPK, INTER = 64, 8, 96
TOK = BATCH * SEQ
NT = TOK // P
DC = D // P
HG = 4
NG = BATCH * H // HG
HALF = DK // 2
PARTS = 3
Q_PART, K_PART = (0, 0, 0, 1, 1, 2), (0, 1, 2, 0, 1, 0)
SROWS = len(Q_PART) * DK
XROWS = SROWS + PARTS
CH = 512
NT_FFN = TOK * TOPK // P + E
GU = 2 * INTER
NEG = -1.0e30
EPS = 1e-5

STEPS = [(c, j) for c in range(2) for j in range(4 * (c + 1))]
EXP = [(c, j, h, max(0, P * j - CH * c)) for c, j in STEPS for h in range(HG)]
MAXU = [(t // 4, t, h, kc, min(CH, P * (t + 1) - CH * kc))
        for t in range(8) for h in range(HG) for kc in range(t // 4 + 1)]
ST_INC = 16 * (2 * len(Q_PART) + 1)
ROW_INC = 16 * HG
N_EXP, N_MAX, N_STEP = len(EXP), len(MAXU), len(STEPS)
N_MAX0 = sum(1 for m in MAXU if m[0] == 0)
MX_RING, EX_RING, P_RING = 4, 2, 3
MX_HEAD = N_MAX + 1
MX_BODY = N_MAX + 2
MROW1_AT = 6
MAX_FROM = 8
MAX_AT = [MAX_FROM + k * (N_EXP - MAX_FROM) // N_MAX for k in range(N_MAX)]
MROW0_AFTER = N_MAX0 + 4


def row_fill(c, g):
    if c == 1:
        return MX_HEAD + MX_BODY * g
    return MX_HEAD + MX_BODY * (g - 1) + 1 + MROW0_AFTER if g else N_MAX


RING = 6


def build(nc, x, lora, w_qkv, w_o, lora_a, lora_ao, lora_b, gate, w_gu, w_d, cos, sin, consts, rowc, out):
    ctx = ExitStack()
    with ctx:
        def sb(name, shape, dt=F32):
            return ctx.enter_context(nc.sbuf_tensor(name, shape, dt))

        def sem(name):
            return ctx.enter_context(nc.semaphore(name))

        def dram(name, shape, dt=F32):
            return nc.dram_tensor(name, shape, dt, kind="Internal").ap()

        qk_parts = dram("qk_parts", (2, PARTS, BATCH * H, DK, SEQ), BF16)
        v_rows = dram("v_rows", (NT, P, H * 32))
        x_sorted = dram("x_sorted", (NT_FFN * P, D))
        y_sorted = dram("y_sorted", (NT_FFN * P, D))

        xs = sb("xs", [P, NT, D])
        ident = sb("ident", [P, P])
        ident_b = sb("ident_b", [P, P], BF16)
        mask_qk = sb("mask_qk", [P, P], BF16)
        mask_kq = sb("mask_kq", [P, P], BF16)
        sel = sb("sel", [P, P])
        wo_eff = sb("wo_eff", [P, BATCH, NG // BATCH, D])
        o_sb = sb("o_sb", [P, NG, SEQ])
        slot_i = sb("slot_i", [P, NT, TOPK], I32)
        w_top = sb("w_top", [P, NT, TOPK])
        tile_e = sb("tile_e", [1, NT_FFN], I32)

        arena = sb("arena", [P, 30 * 1024])

        def cut(at, n, shape=None, dt=F32):
            v = arena[:, at:at + n]
            if dt != F32:
                v = v.bitcast(dt)
            return v if shape is None else v.rearrange(shape[0], **shape[1])

        xn = cut(0, 4096, ("p (t d) -> p t d", dict(d=D)))
        xnT = cut(4096, 4096, ("p (c t) -> p c t", dict(c=DC)))
        w_in = cut(8192, 1536, ("p (w c o) -> p w c o", dict(w=3, c=DC)))
        w_eff = cut(9728, 3072, ("p (b w c o) -> p b w c o", dict(b=BATCH, w=3, c=DC)))
        wo_in = cut(12800, 1024, ("p (g o) -> p g o", dict(g=4)))
        la = cut(13824, 768, ("p (w d) -> p w d", dict(w=3)))
        lao = cut(14592, 512, ("p (g d) -> p g d", dict(g=4)))
        lb = cut(15104, 1024, ("p (w o) -> p w o", dict(w=4)))
        lbs = cut(16128, 2048, ("p (b w o) -> p b w o", dict(b=BATCH, w=4)))
        cs = cut(18176, 1024)
        sn = cut(19200, 1024)
        gw = cut(20224, 128, ("p (c e) -> p c e", dict(c=DC)))
        cin = cut(20352, 1024, ("p (k m) -> p k m", dict(k=8)))
        tri_b = cut(21376, 64, dt=BF16)
        ones_b = cut(21440, 64, dt=BF16)
        vst = cut(21504, 1024, ("p (r h d) -> p r h d", dict(r=2, h=H)))
        t1 = cut(22528, 1024, ("p (a q) -> p a q", dict(a=2)))
        t2 = cut(23552, 1024, ("p (a q) -> p a q", dict(a=2)))
        oo = cut(24576, 1024, ("p (a q) -> p a q", dict(a=2)))
        rr = cut(25600, 1024, ("p (a q) -> p a q", dict(a=2)))
        pp = [[cut(26624 + 512 * (3 * r + k), 512, ("p (a q) -> p a q", dict(a=2)), BF16)
               for k in range(PARTS)] for r in range(2)]
        logit = sb("logit", [P, NT, E])
        chosen = sb("chosen", [P, NT, E])
        chosen_b = sb("chosen_b", [P, NT, E], BF16)
        before_b = sb("before_b", [P, NT + 1, E], BF16)
        slot = sb("slot", [P, NT, E])
        wts = sb("wts", [P, NT, E])
        tmp = cut(22528, 1024, ("p (t e) -> p t e", dict(t=NT)))
        before = cut(23552, 1088, ("p (t e) -> p t e", dict(t=NT + 1)))
        top8 = cut(24704, 128, ("p (t k) -> p t k", dict(t=NT)))
        stop8 = cut(24832, 128, ("p (t k) -> p t k", dict(t=NT)))
        small = cut(24960, 640)
        tcmp_b = cut(25600, 96, dt=BF16)
        stats = sb("stats", [P, NT, 6])
        mv = sb("mv", [P, NT, 2])
        rstd = sb("rstd", [P, 4, NT])
        iota_t = sb("iota_t", [E, NT_FFN + 2])
        onehot = sb("onehot", [E, 16])
        starts = sb("starts", [E, N_LORA], I32)
        zeros = o_sb[:, 0:2, :].rearrange("p g t -> p (g t)")

        q_st = [cut(4096 + 2048 * u, 2048, ("p (h t) -> p h t", dict(h=HG)), BF16) for u in range(2)]
        k_st = [cut(8192 + 2048 * u, 2048, ("p (h t) -> p h t", dict(h=HG)), BF16) for u in range(2)]
        v_st = [cut(12288 + 1024 * u, 1024, ("p (j h d) -> p j h d", dict(j=8, h=HG))) for u in range(2)]
        probs = [cut(14336 + 2048 * u, 2048, ("p (h q) -> p h q", dict(h=HG))) for u in range(P_RING)]
        m_row = [cut(20480 + 256 * c, 256, dt=BF16) for c in range(2)]
        mx = [[cut(20992 + 32 * c + 16 * k, 16, ("p (t h) -> p t h", dict(t=4))) for k in range(2)] for c in range(2)]
        m_all = cut(21056, 16, ("p (t h) -> p t h", dict(t=4)))
        m_res = cut(21072, 16, ("p (t h) -> p t h", dict(t=4)))
        m_parts = [cut(21088 + 24 * c, 24, ("p (t h s) -> p t h s", dict(t=4, s=PARTS)), BF16) for c in range(2)]
        base = 21504
        fx = [cut(base + 256 * r, 256) for r in range(RING)]
        fw = [cut(base + 1536 + 384 * r, 384, ("p (c i) -> p c i", dict(c=DC))) for r in range(RING)]
        fd = [cut(base + 5376 + 256 * r, 256)[0:INTER, :] for r in range(RING)]
        fxT = [cut(base + 6912 + 256 * r, 256, ("p (c t) -> p c t", dict(c=DC))) for r in range(2)]
        fth = [cut(base + 7424 + 96 * r, 96) for r in range(2)]
        fz = [cut(base + 7616 + 96 * r, 96) for r in range(2)]
        fa = [cut(base + 7808 + 96 * r, 96) for r in range(2)]
        fzT = [cut(base + 8000 + 128 * r, 128)[0:INTER, :] for r in range(2)]
        fy = [cut(base + 3840 + 256 * r, 256) for r in range(RING)]
        YG = 12
        rec = [cut(CH * r, CH) for r in range(2)]
        yg = [cut(1024 + 256 * r, 256) for r in range(YG)]

        ps = ctx.enter_context(nc.psum_tensor("ps", [P, 8, CH], F32))
        MX = [ps[:, k, :] for k in range(4)]
        EX = [ps[:, 4 + k, :] for k in range(2)]
        PV = [ps[:, 6 + c, :] for c in range(2)]

        const_in, lora_in, x_in0 = sem("const_in"), sem("lora_in"), [sem(f"x_in{k}") for k in range(4)]
        const_ok, dve_step, act_step = sem("const_ok"), sem("dve_step"), sem("act_step")
        zero_ok, filled = sem("zero_ok"), sem("filled")
        var_ok, std_ok, xn_ok = sem("var_ok"), sem("std_ok"), sem("xn_ok")
        xt_ps, xt_ok = sem("xt_ps"), sem("xt_ok")
        lora_ps, w_ok, b_ok = sem("lora_ps"), sem("w_ok"), sem("b_ok")
        vl_ps, v_ok, logit_ok = sem("vl_ps"), sem("v_ok"), sem("logit_ok")
        v_out = [sem(f"v_out{r}") for r in range(2)]
        qk_ps, rope_free, rot_ok, p1_ok = sem("qk_ps"), sem("rope_free"), sem("rot_ok"), sem("p1_ok")
        r_ok, p2_ok, p3_ok = sem("r_ok"), sem("p2_ok"), sem("p3_ok")
        parts_out = [sem(f"parts_out{r}") for r in range(2)]
        exp_in, exp_out, before_ok = sem("exp_in"), sem("exp_out"), sem("before_ok")
        rank_ps, tcol_ok, te_ps, route_ok = sem("rank_ps"), sem("tcol_ok"), sem("te_ps"), sem("route_ok")
        sorted_ok = sem("sorted_ok")
        minus_ok = sem("minus_ok")
        st_in = [sem(f"st_in{u}") for u in range(2)]
        mx_full, mx_done, ex_full, ex_done = sem("mx_full"), sem("mx_done"), sem("ex_full"), sem("ex_done")
        pv_done, pv_copied, m_ok, m_step = sem("pv_done"), sem("pv_copied"), sem("m_ok"), sem("m_step")
        mrow_in = [sem(f"mrow_in{c}") for c in range(2)]
        f_in = [sem(f"f_in{r}") for r in range(RING)]
        y_out = [sem(f"y_out{r}") for r in range(RING)]
        fxt_ps, fxt_ok, gu_ps, th_ok = sem("fxt_ps"), sem("fxt_ok"), sem("gu_ps"), sem("th_ok")
        fa_ok, z_ok, zt_ps, zt_ok = sem("fa_ok"), sem("z_ok"), sem("zt_ps"), sem("zt_ok")
        y_ps, y_ok = sem("y_ps"), sem("y_ok")
        yg_in = [sem(f"yg_in{r}") for r in range(YG)]
        den_ps, rec_ok, o_ok, pr_ps = sem("den_ps"), sem("rec_ok"), sem("o_ok"), sem("pr_ps")
        attn_ok, moe_step, out_done = sem("attn_ok"), sem("moe_step"), sem("out_done")

        QK = [(b, c, w) for b in range(BATCH) for c in range(2) for w in range(2)]
        block = ctx.enter_context(nc.Block())

        @block.sync
        def _(sp):
            def ffn_loads():
                sp.wait_ge(route_ok, 1)
                sp.wait_ge(sorted_ok, 16 * NT * TOPK)
                xv = x_sorted.rearrange("(t p) d -> t p d", p=P)
                yv = y_sorted.rearrange("(t p) d -> t p d", p=P)

                def load(t, r):
                    e = sp.value_load(tile_e[0:1, bass.ds(t, 1)], min_val=0, max_val=E - 1)
                    sp.dma_start(fx[r], xv[bass.ds(t, 1)].rearrange("a p d -> (a p) d")).then_inc(f_in[r], 16)
                    sp.dma_start(fw[r].rearrange("p c i -> p (c i)"), w_gu[bass.ds(e, 1)].rearrange("a p i -> (a p) i")).then_inc(f_in[r], 16)
                    sp.dma_start(fd[r][:, :], w_d[bass.ds(e, 1)].rearrange("a p i -> (a p) i")).then_inc(f_in[r], 16)

                def store(t, r):
                    sp.dma_start(yv[bass.ds(t, 1)].rearrange("a p d -> (a p) d"), fy[r]).then_inc(y_out[r], 16)

                for r in range(RING):
                    load(r, r)
                with sp.Fori(1, NT_FFN // RING) as i:
                    for r in range(RING):
                        t = i * RING + r
                        sp.wait_ge(y_ps, t - RING + 1)
                        load(t, r)
                        sp.wait_ge(y_ok, t - RING + 1)
                        store(t - RING, r)
                for r in range(RING):
                    t = NT_FFN - RING + r
                    sp.wait_ge(y_ok, t + 1)
                    store(t, r)

            for s in mrow_in + y_out:
                sp.sem_inc(s, 16)
            xv = x.rearrange("(t p) d -> p t d", p=P)
            for k in range(4):
                sp.dma_start(xs[:, 4 * k:4 * k + 4, :], xv[:, 4 * k:4 * k + 4, :]).then_inc(x_in0[k], 16)
            sp.dma_start(cin[:, :, :], consts).then_inc(const_in, 16)
            sp.dma_start(iota_t[:, :], rowc).then_inc(const_in, 16)
            sp.dma_start(starts[:, :], lora.partition_broadcast(E)).then_inc(lora_in, 16)
            sp.dma_start(lb[0:E, :, :], lora_b).then_inc(lora_in, 16)
            sp.dma_start(la[0:E, :, :], lora_a).then_inc(lora_in, 16)
            sp.dma_start(lao[0:E, :, :], lora_ao).then_inc(lora_in, 16)
            sp.dma_start(w_in[:, :, :, :], w_qkv).then_inc(lora_in, 16)
            sp.dma_start(wo_in[:, :, :], w_o).then_inc(lora_in, 16)
            sp.dma_start(gw[:, :, :], gate).then_inc(lora_in, 16)
            sp.dma_start(cs, cos).then_inc(const_in, 16)
            sp.dma_start(sn, sin).then_inc(const_in, 16)

            sp.wait_ge(zero_ok, 1)
            per = NT_FFN * P // P
            fill = x_sorted.rearrange("(p r) d -> p r d", p=P)
            for k in range(per // 8):
                sp.dma_start(fill[:, 8 * k:8 * k + 8, :].rearrange("p r d -> p (r d)"), zeros).then_inc(filled, 16)

            for t in range(NT):
                sp.wait_ge(v_ok, t + 1)
                sp.dma_start(v_rows[t], vst[:, t % 2, :, :].rearrange("p h d -> p (h d)")).then_inc(v_out[t % 2], 16)

            for n, (b, c, w) in enumerate(QK):
                sp.wait_ge(p3_ok, n + 1)
                for k in range(PARTS):
                    for a in range(2):
                        dst = qk_parts[w, k, b * H:(b + 1) * H, a * HALF:(a + 1) * HALF, c * CH:(c + 1) * CH]
                        sp.dma_start(dst, pp[n % 2][k][:, a, :]).then_inc(parts_out[n % 2], 16)
            for r in range(2):
                sp.wait_ge(parts_out[r], 16 * 6 * 4)
                sp.wait_ge(v_out[r], 16 * 8)

            def load_group(g, u):
                for w, st, order in ((0, q_st, Q_PART), (1, k_st, K_PART)):
                    for s, part in enumerate(order):
                        src = qk_parts[w, part, bass.ds(g * HG, HG), :, :].rearrange("h r t -> r h t")
                        sp.dma_start(st[u][s * DK:(s + 1) * DK, :, :], src).then_inc(st_in[u], 16)

            def group(g, u, v_src):
                load_group(g, u)
                sp.dma_start(v_st[u][:, :, :, :].rearrange("p j h d -> p j (h d)"), v_src).then_inc(st_in[u], 16)

            def v_of(g):
                b, hg = divmod(g, 4)
                return v_rows[8 * b:8 * b + 8, :, hg * 128:(hg + 1) * 128].rearrange("t p w -> p t w")

            def put_row(c, g):
                sp.wait_ge(mx_done, row_fill(c, g) + 1)
                u = g % 2
                for h in range(HG):
                    sp.dma_start(q_st[u][SROWS:XROWS, h, c * CH:(c + 1) * CH],
                                 m_row[c][PARTS * h:PARTS * (h + 1), :]).then_inc(mrow_in[c], 16)

            group(0, 0, v_of(0))
            put_row(0, 0)
            for g in range(NG):
                if g + 1 < NG:
                    if g:
                        sp.wait_ge(pv_done, N_STEP * g + P_RING)
                    group(g + 1, (g + 1) % 2, v_of(g + 1))
                put_row(1, g)
                if g + 1 < NG:
                    put_row(0, g + 1)
                if g == NG - 3:
                    ffn_loads()

            ov = out.rearrange("(t p) d -> p t d", p=P)
            for t in range(NT):
                sp.wait_ge(moe_step, TOPK * (t + 1))
                sp.dma_start(ov[:, t, :], xs[:, t, :]).then_inc(out_done, 16)
            sp.wait_ge(out_done, 16 * NT)

        @block.gpsimd
        def _(pool):
            nc.gpsimd.memset(zeros, 0.0).then_inc(zero_ok, 1)
            nc.gpsimd.memset(vst[:, :, :, :], 1.0).then_inc(zero_ok, 1)
            for n in range(len(QK)):
                pool.wait_ge(p2_ok, n + 1)
                nc.gpsimd.tensor_tensor(pp[n % 2][2][:, :, :], rr[:, :, :], pp[n % 2][1][:, :, :],
                                        ALU.subtract).then_inc(p3_ok, 1)
            pool.wait_ge(route_ok, 1)
            pool.wait_ge(filled, 16 * (NT_FFN // 8))
            pool.wait_ge(xn_ok, NT)
            for t in range(NT):
                for k in range(TOPK):
                    nc.gpsimd.indirect_dma_start(
                        out=x_sorted, out_offset=bass.IndirectOffsetOnAxis(ap=slot_i[:, t, k:k + 1], axis=0),
                        in_=xn[:, t, :], in_offset=None).then_inc(sorted_ok, 16)
            for r in range(RING):
                pool.wait_ge(y_out[r], 16 * (NT_FFN // RING) + 16)
            for n in range(NT * TOPK):
                t, k = divmod(n, TOPK)
                if n >= YG:
                    pool.wait_ge(moe_step, n - YG + 1)
                nc.gpsimd.indirect_dma_start(
                    out=yg[n % YG], out_offset=None, in_=y_sorted,
                    in_offset=bass.IndirectOffsetOnAxis(ap=slot_i[:, t, k:k + 1], axis=0)).then_inc(yg_in[n % YG], 16)

        @block.scalar
        def _(act):
            act.wait_ge(var_ok, 1)
            nc.scalar.activation(rstd[:, 1, :], rstd[:, 0, :], ACT.Sqrt).then_inc(std_ok, 1)
            for n in range(NT // 2):
                act.wait_ge(xt_ps, n + 1)
                nc.scalar.activation(
                    xnT[:, :, 2 * P * n:2 * P * (n + 1)].rearrange("p c (a t) -> p a c t", a=2),
                    ps[:, n % 2, :].rearrange("p (a c t) -> p a c t", a=2, c=DC), ACT.Copy).then_inc(xt_ok, 1)
            act.wait_ge(zero_ok, 2)
            for t in range(NT):
                act.wait_ge(vl_ps, t + 1)
                if t >= 2:
                    act.wait_ge(v_out[t % 2], 16 * (t // 2))
                nc.scalar.activation(vst[:, t % 2, :, 0:DK],
                                     ps[:, t % 4, 0:D].rearrange("p (h d) -> p h d", h=H), ACT.Copy).then_inc(v_ok, 1)
            for n in range(len(QK)):
                act.wait_ge(rot_ok, n + 1)
                if n >= 2:
                    act.wait_ge(parts_out[n % 2], 16 * 6 * (n // 2))
                nc.scalar.activation(pp[n % 2][0][:, :, :], oo[:, :, :], ACT.Copy).then_inc(p1_ok, 1)
                act.wait_ge(r_ok, n + 1)
                nc.scalar.activation(pp[n % 2][1][:, :, :], rr[:, :, :], ACT.Copy).then_inc(p2_ok, 1)
            act.wait_ge(exp_in, 1)
            nc.scalar.activation(wts[:, :, :], tmp[:, :, :], ACT.Exp).then_inc(exp_out, 1)

            act.wait_ge(filled, 16 * (NT_FFN // 8))
            act.sem_inc(ex_done, EX_RING)
            act.sem_inc(pv_copied, 2)

            def group(g):
                for n, (c, j, h, off) in enumerate(EXP):
                    s = n // HG
                    act.wait_ge(ex_full, g * N_EXP + n + 1)
                    if n % HG == 0:
                        act.wait_ge(pv_done, g * N_STEP + s + 1)
                    nc.scalar.activation(probs[s % P_RING][:, h, off:CH], EX[n % EX_RING][:, off:CH], ACT.Exp,
                                         scale=0.25).then_inc(ex_done, 1)
                    if n == N_MAX0 + 6:
                        copy_pv(g, 0)
                copy_pv(g, 1)

            def copy_pv(g, c):
                act.wait_ge(pv_done, g * N_STEP + (4 if c == 0 else N_STEP) + P_RING)
                nc.scalar.activation(o_sb[:, bass.ds(g, 1), c * CH:(c + 1) * CH].rearrange("p a q -> p (a q)"),
                                     PV[c], ACT.Copy).then_inc(pv_copied, 1)

            with act.Fori(0, NG // 2 - 1) as i:
                for u in range(2):
                    group(i * 2 + u)

            def slot_work(s, k):
                static = isinstance(s, int)
                if not static or s < NT_FFN:
                    act.wait_ge(fxt_ps, s + 1)
                    if not static or s >= 2:
                        act.wait_ge(gu_ps, s - 1)
                    nc.scalar.activation(fxT[k % 2][:, :, :], ps[:, k % 2, 0:D].rearrange("p (c t) -> p c t", c=DC),
                                         ACT.Copy).then_inc(fxt_ok, 1)
                if not static or 1 <= s < NT_FFN + 1:
                    t = s - 1
                    act.wait_ge(gu_ps, t + 1)
                    if not static or t >= 2:
                        act.wait_ge(z_ok, t - 1)
                    nc.scalar.activation(fth[(k - 1) % 2][:, :], ps[:, 2 + (k - 1) % 2, 0:INTER], ACT.Tanh,
                                         scale=0.5).then_inc(th_ok, 1)
                if not static or 3 <= s < NT_FFN + 3:
                    t = s - 3
                    act.wait_ge(y_ps, t + 1)
                    if static and t >= RING:
                        act.wait_ge(y_out[t % RING], 16 * (t // RING) + 16)
                    elif not static:
                        act.wait_ge(y_out[(k - 3) % RING], (turn[0] - (k % RING < 3)) * 16 + 16)
                    nc.scalar.activation(fy[(k - 3) % RING], ps[:, 6 + (k - 3) % 2, 0:D], ACT.Copy).then_inc(y_ok, 1)

            turn = [0]
            for s in range(RING):
                slot_work(s, s)
            with act.Fori(1, NT_FFN // RING) as i:
                turn[0] = i
                for r in range(RING):
                    slot_work(i * RING + r, r + RING)
            for s in range(NT_FFN, NT_FFN + 3):
                slot_work(s, s)

            for g in (NG - 2, NG - 1):
                group(g)

        @block.tensor
        def _(pe):
            pe.wait_ge(const_ok, 1)
            for n in range(NT // 2):
                pe.wait_ge(xn_ok, 2 * n + 2)
                if n >= 2:
                    pe.wait_ge(xt_ok, n - 1)
                for a in range(2):
                    for c in range(DC):
                        at = (a * DC + c) * P
                        mm = nc.tensor.transpose(ps[:, n % 2, at:at + P], xn[:, 2 * n + a, c * P:(c + 1) * P], ident[:, :])
                mm.then_inc(xt_ps, 1)
            n = 0
            pe.wait_ge(lora_in, 16 * 7)
            for b in range(BATCH):
                pe.wait_ge(b_ok, b + 1)
                for w in range(5):
                    if n >= 2:
                        pe.wait_ge(w_ok, n - 1)
                    for c in range(2):
                        if w < 3:
                            lhsT, rhs = la[0:E, w, c * P:(c + 1) * P], lbs[0:E, b, w, :]
                        else:
                            lhsT, rhs = lao[0:E, 2 * (w - 3) + c, :], lbs[0:E, b, 3, :]
                        mm = nc.tensor.matmul(ps[:, 2 + n % 2, c * D:(c + 1) * D], lhsT, rhs, start=True, stop=True)
                    mm.then_inc(lora_ps, 1)
                    n += 1
            pe.wait_ge(xt_ok, NT // 2)
            pe.wait_ge(w_ok, 10)
            for t in range(NT):
                if t >= 4:
                    pe.wait_ge(v_ok, t - 3)
                    pe.wait_ge(logit_ok, t - 3)
                for c in range(DC):
                    nc.tensor.matmul(ps[:, t % 4, 0:D], xnT[:, c, t * P:(t + 1) * P], w_eff[:, t // 8, 2, c, :],
                                     start=(c == 0), stop=(c == DC - 1))
                for c in range(DC):
                    mm = nc.tensor.matmul(ps[:, t % 4, D:D + E], xnT[:, c, t * P:(t + 1) * P], gw[:, c, :],
                                          start=(c == 0), stop=(c == DC - 1))
                mm.then_inc(vl_ps, 1)
            for n, (b, ch, w) in enumerate(QK):
                if n >= 2:
                    pe.wait_ge(rope_free, n - 1)
                at = b * SEQ + ch * CH
                for a in range(2):
                    for c in range(DC):
                        mm = nc.tensor.matmul(ps[:, 4 + 2 * (n % 2) + a, :], w_eff[:, b, w, c, a * P:(a + 1) * P],
                                              xnT[:, c, at:at + CH], start=(c == 0), stop=(c == DC - 1))
                mm.then_inc(qk_ps, 1)
            pe.wait_ge(v_ok, NT)
            pe.wait_ge(before_ok, 1)
            for t in range(NT):
                at = ps[:, t // 8, (t % 8) * E:(t % 8 + 1) * E]
                nc.tensor.matmul(at, tri_b, chosen_b[:, t, :], start=True, stop=False)
                nc.tensor.matmul(at, ones_b, before_b[:, t, :], start=False, stop=True)
            nc.tensor.matmul(ps[:, 2, 0:E], ones_b, before_b[:, NT, :], start=True, stop=True).then_inc(rank_ps, 1)
            pe.wait_ge(tcol_ok, 1)
            nc.tensor.matmul(ps[0:1, 3, 0:NT_FFN], ones_b[0:E, 0:1], tcmp_b[0:E, 0:NT_FFN],
                             start=True, stop=True).then_inc(te_ps, 1)
            pe.wait_ge(route_ok, 1)

            pe.sem_inc(pv_done, P_RING)
            pe.wait_ge(minus_ok, 1)

            def max_unit(k, fill, slot_, u, wait):
                c, t, h, kc, w = MAXU[k]
                if wait:
                    pe.wait_ge(mx_done, fill - MX_RING + 1)
                o = MX[slot_ % MX_RING][:, 0:w]
                diag = kc == t // 4
                mm = nc.tensor.matmul(o, q_st[u][0:SROWS, h, t * P:(t + 1) * P], k_st[u][0:SROWS, h, kc * CH:kc * CH + w],
                                      start=True, stop=not diag)
                if diag:
                    mm = nc.tensor.matmul(o[:, w - P:w], ident_b[:, :], mask_qk[:, :], start=False, stop=True)
                mm.then_inc(mx_full, 1)

            def max_row(c, fill, slot_, n_ready, wait=True):
                pe.wait_ge(m_ok, n_ready)
                pe.wait_ge(mx_done, fill - MX_RING + 1)
                o = MX[slot_ % MX_RING].bitcast(BF16)
                for t in range(4):
                    mm = nc.tensor.transpose(o[0:12, t * P:(t + 1) * P], m_parts[c][:, t, :, :].rearrange("p h s -> p (h s)"),
                                             ident_b[:, :])
                mm.then_inc(mx_full, 1)

            def pv(g, s, u):
                c, j = STEPS[s]
                off = max(0, P * j - CH * c)
                pe.wait_ge(ex_done, g * N_EXP + HG * (s + 1) + EX_RING)
                if j == 0:
                    pe.wait_ge(pv_copied, g * 2 + c + 1)
                for h in range(HG):
                    mm = nc.tensor.matmul(PV[c][32 * h:32 * h + 32, off:CH], v_st[u][:, j, h, :],
                                          probs[s % P_RING][:, h, off:CH], start=(j == 0), stop=(j == 4 * c + 3),
                                          skip_group_check=True)
                mm.then_inc(pv_done, 1)

            def group(i, u, last=False):
                g = i * 2 + u
                fill = g * MX_BODY + MX_HEAD
                slot_ = MX_HEAD + MX_BODY * u
                k = 0
                for n, (c, j, h, off) in enumerate(EXP):
                    if n == 0:
                        pe.wait_ge(mrow_in[0], (g + 1) * ROW_INC + 16)
                    if n == N_MAX0:
                        pe.wait_ge(mrow_in[1], (g + 1) * ROW_INC + 16)
                    pe.wait_ge(ex_done, g * N_EXP + n + 1)
                    o = EX[n % EX_RING]
                    diag = P * j >= CH * c
                    mm = nc.tensor.matmul(o[:, off:CH], k_st[u][0:XROWS, h, j * P:(j + 1) * P],
                                          q_st[u][0:XROWS, h, c * CH + off:(c + 1) * CH], start=True, stop=not diag)
                    if diag:
                        mm = nc.tensor.matmul(o[:, off:off + P], ident_b[:, :], mask_kq[:, :], start=False, stop=True)
                    mm.then_inc(ex_full, 1)
                    if n == MROW1_AT:
                        max_row(1, fill, slot_, g * 2 + 2)
                        fill, slot_ = fill + 1, slot_ + 1
                    while not last and k < N_MAX and MAX_AT[k] == n:
                        if k == 0:
                            pe.wait_ge(st_in[1 - u], (i + 1 + u) * ST_INC)
                        if k == MROW0_AFTER:
                            max_row(0, fill, slot_, g * 2 + 3)
                            fill, slot_ = fill + 1, slot_ + 1
                        max_unit(k, fill, slot_, 1 - u, True)
                        fill, slot_, k = fill + 1, slot_ + 1, k + 1
                    if n % HG == HG - 1 and n >= HG:
                        pv(g, n // HG - 1, u)
                pv(g, N_STEP - 1, u)

            pe.wait_ge(st_in[0], ST_INC)
            fill = 0
            for k in range(N_MAX):
                max_unit(k, fill, fill, 0, fill >= MX_RING)
                fill += 1
                if k == N_MAX - 1:
                    max_row(0, fill, fill, 1)
                    fill += 1
            with pe.Fori(0, NG // 2 - 1) as i:
                for u in range(2):
                    group(i, u)

            def slot_work(s, k):
                static = isinstance(s, int)
                if not static or s < NT_FFN:
                    pe.wait_ge(f_in[k % RING], (turn[0] + 1) * 48)
                    if not static or s >= 2:
                        pe.wait_ge(fxt_ok, s - 1)
                    for c in range(DC):
                        mm = nc.tensor.transpose(ps[:, k % 2, c * P:(c + 1) * P], fx[k % RING][:, c * P:(c + 1) * P], ident[:, :])
                    mm.then_inc(fxt_ps, 1)
                if not static or 1 <= s < NT_FFN + 1:
                    t, kt = s - 1, k - 1
                    pe.wait_ge(fxt_ok, t + 1)
                    if not static or t >= 2:
                        pe.wait_ge(z_ok, t - 1)
                    for c in range(DC):
                        mm = nc.tensor.matmul(ps[:, 2 + kt % 2, 0:GU], fxT[kt % 2][:, c, :], fw[kt % RING][:, c, :],
                                              start=(c == 0), stop=(c == DC - 1))
                    mm.then_inc(gu_ps, 1)
                if not static or 2 <= s < NT_FFN + 2:
                    t, kt = s - 2, k - 2
                    pe.wait_ge(z_ok, t + 1)
                    if not static or t >= 2:
                        pe.wait_ge(zt_ok, t - 1)
                    nc.tensor.transpose(ps[0:INTER, 4 + kt % 2, 0:P], fz[kt % 2][:, :], ident[:, :]).then_inc(zt_ps, 1)
                if not static or 3 <= s < NT_FFN + 3:
                    t, kt = s - 3, k - 3
                    pe.wait_ge(zt_ok, t + 1)
                    if not static or t >= 2:
                        pe.wait_ge(y_ok, t - 1)
                    nc.tensor.matmul(ps[:, 6 + kt % 2, 0:D], fzT[kt % 2][:, :], fd[kt % RING][:, :],
                                     start=True, stop=True).then_inc(y_ps, 1)

            turn = [0]
            pe.wait_ge(mx_done, MX_HEAD + MX_BODY * (NG - 2))
            pe.wait_ge(pv_copied, 2 * (NG - 2) + 2)
            for s in range(RING):
                slot_work(s, s)
            with pe.Fori(1, NT_FFN // RING) as i:
                turn[0] = i
                for r in range(RING):
                    slot_work(i * RING + r, r + RING)
            for s in range(NT_FFN, NT_FFN + 3):
                slot_work(s, s)
            pe.wait_ge(y_ok, NT_FFN)

            group(NG // 2 - 1, 0)
            group(NG // 2 - 1, 1, last=True)

            n = 0
            for g in range(NG):
                for c in range(2):
                    if n == 0:
                        pe.wait_ge(mx_done, MX_HEAD + MX_BODY * (NG - 1) + 1)
                    pe.wait_ge(pv_copied, 2 * g + c + 3)
                    if n >= 2:
                        pe.wait_ge(rec_ok, n - 1)
                    nc.tensor.matmul(ps[:, n % 2, :], sel[:, :], o_sb[:, g, c * CH:(c + 1) * CH],
                                     start=True, stop=True).then_inc(den_ps, 1)
                    n += 1
                if g % 4 == 3:
                    b = g // 4
                    for t in range(8):
                        m = 8 * b + t
                        if t % 4 == 0:
                            pe.wait_ge(o_ok, 8 * b + 8)
                        if m >= 2:
                            pe.wait_ge(attn_ok, m - 1)
                        for k in range(4):
                            mm = nc.tensor.matmul(ps[:, 2 + m % 2, 0:D], o_sb[:, 4 * b + k, t * P:(t + 1) * P],
                                                  wo_eff[:, b, k, :], start=(k == 0), stop=(k == 3))
                        mm.then_inc(pr_ps, 1)

        @block.vector
        def _(dve):
            step = [0]

            def link(ins):
                step[0] += 1
                ins.then_inc(dve_step, 1)
                dve.wait_ge(dve_step, step[0])

            dve.wait_ge(const_in, 64)
            nc.vector.tensor_copy(ident[:, :], cin[:, 0, :])
            nc.vector.tensor_copy(ident_b[:, :], cin[:, 0, :])
            nc.vector.tensor_copy(mask_qk[:, :], cin[:, 1, :])
            nc.vector.tensor_copy(mask_kq[:, :], cin[:, 2, :])
            nc.vector.tensor_copy(sel[:, :], cin[:, 3, :])
            nc.vector.tensor_copy(tri_b, cin[:, 4, :])
            nc.vector.tensor_copy(ones_b, cin[:, 5, :]).then_inc(const_ok, 1)

            for t in range(NT):
                if t % 4 == 0:
                    dve.wait_ge(x_in0[t // 4], 16)
                ins = nc.vector.bn_stats(stats[:, t, :], xs[:, t, :])
            link(ins)
            for t in range(NT):
                ins = nc.vector.bn_aggr(mv[:, t, :], stats[:, t, :])
            link(ins)
            nc.vector.tensor_scalar(rstd[:, 0, :], mv[:, :, 1], EPS, None, ALU.add).then_inc(var_ok, 1)
            dve.wait_ge(std_ok, 1)
            link(nc.vector.reciprocal(rstd[:, 2, :], rstd[:, 1, :]))
            link(nc.vector.tensor_tensor(rstd[:, 1, :], rstd[:, 2, :], rstd[:, 2, :], ALU.mult))
            link(nc.vector.tensor_tensor(rstd[:, 1, :], rstd[:, 1, :], rstd[:, 0, :], ALU.mult))
            link(nc.vector.tensor_scalar(rstd[:, 1, :], rstd[:, 1, :], -0.5, 1.5, ALU.mult, ALU.add))
            link(nc.vector.tensor_tensor(rstd[:, 3, :], rstd[:, 2, :], rstd[:, 1, :], ALU.mult))
            for t in range(NT):
                nc.vector.tensor_scalar(xn[:, t, :], xs[:, t, :], mv[:, t, 0:1], rstd[:, 3, t:t + 1],
                                        ALU.subtract, ALU.mult).then_inc(xn_ok, 1)

            dve.wait_ge(lora_in, 16 * 7)
            oh = lambda a, b: onehot[:, a:b]
            link(nc.vector.tensor_copy(oh(0, 4), starts[:, :]))
            for b in range(BATCH):
                link(nc.vector.tensor_scalar(oh(4, 8), oh(0, 4), float(b), None, ALU.is_le))
                link(nc.vector.tensor_reduce(oh(8, 9), oh(4, 8), AX, ALU.add))
                link(nc.vector.tensor_scalar(oh(9, 10), oh(8, 9), -1.0, 0.0, ALU.add, ALU.max))
                link(nc.vector.tensor_scalar(oh(10, 11), oh(9, 10), float(N_LORA - 1), iota_t[:, NT_FFN:NT_FFN + 1],
                                             ALU.min, ALU.is_equal))
                nc.vector.tensor_scalar(lbs[0:E, b, :, :], lb[0:E, :, :], oh(10, 11), None, ALU.mult).then_inc(b_ok, 1)
            n = 0
            for b in range(BATCH):
                for w in range(5):
                    dve.wait_ge(lora_ps, n + 1)
                    o, i = (w_eff[:, b, w, :, :], w_in[:, w, :, :]) if w < 3 else \
                        (wo_eff[:, b, 2 * (w - 3):2 * (w - 3) + 2, :], wo_in[:, 2 * (w - 3):2 * (w - 3) + 2, :])
                    nc.vector.tensor_tensor(o, ps[:, 2 + n % 2, :].rearrange("p (c o) -> p c o", c=2), i,
                                            ALU.add).then_inc(w_ok, 1)
                    n += 1
            for t in range(NT):
                dve.wait_ge(vl_ps, t + 1)
                dve.wait_ge(v_ok, t + 1)
                nc.vector.tensor_copy(logit[:, t, :], ps[:, t % 4, D:D + E]).then_inc(logit_ok, 1)

            for n, (b, c, w) in enumerate(QK):
                dve.wait_ge(qk_ps, n + 1)
                src = ps[:, 4 + 2 * (n % 2):6 + 2 * (n % 2), :]
                tab = lambda v: v[:, c * CH:(c + 1) * CH].unsqueeze(1).broadcast_to([P, 2, CH])
                nc.vector.tensor_tensor(t1[:, :, :], src, tab(cs), ALU.mult)
                ins = nc.vector.tensor_tensor(t2[:, :, :], src, tab(sn), ALU.mult)
                ins.then_inc(rope_free, 1)
                dve.wait_ge(rope_free, n + 1)
                nc.vector.tensor_tensor(oo[:, 0, :], t1[:, 0, :], t2[:, 1, :], ALU.subtract)
                nc.vector.tensor_tensor(oo[:, 1, :], t2[:, 0, :], t1[:, 1, :], ALU.add).then_inc(rot_ok, 1)
                dve.wait_ge(p1_ok, n + 1)
                if n:
                    dve.wait_ge(p3_ok, n)
                nc.vector.tensor_tensor(rr[:, :, :], oo[:, :, :], pp[n % 2][0][:, :, :], ALU.subtract).then_inc(r_ok, 1)
            dve.wait_ge(p3_ok, len(QK))

            for t in range(NT):
                ins = nc.vector.max(top8[:, t, :], logit[:, t, :])
            link(ins)
            nc.vector.tensor_tensor(tmp[:, :, :], logit[:, :, :], top8[:, :, 0:1].broadcast_to([P, NT, E]),
                                    ALU.subtract).then_inc(exp_in, 1)
            for t in range(NT):
                ins = nc.vector.match_replace(slot[:, t, :], top8[:, t, :], logit[:, t, :], -3.0e38)
            link(ins)
            link(nc.vector.tensor_tensor(chosen[:, :, :], slot[:, :, :], logit[:, :, :], ALU.not_equal))
            nc.vector.tensor_copy(chosen_b[:, :, :], chosen[:, :, :])
            link(nc.vector.memset(before[:, 0, :], 0.0))
            for t in range(NT):
                link(nc.vector.tensor_tensor(before[:, t + 1, :], before[:, t, :], chosen[:, t, :], ALU.add))
            nc.vector.tensor_copy(before_b[:, :, :], before[:, :, :]).then_inc(before_ok, 1)
            dve.wait_ge(exp_out, 1)
            link(nc.vector.tensor_tensor(wts[:, :, :], wts[:, :, :], chosen[:, :, :], ALU.mult))
            link(nc.vector.tensor_reduce(small[:, 0:NT], wts[:, :, :], AX, ALU.add))
            link(nc.vector.reciprocal(small[:, 16:32], small[:, 0:NT]))
            link(nc.vector.tensor_scalar(small[:, 32:48], small[:, 16:32], 0.5, None, ALU.mult))
            link(nc.vector.tensor_tensor(wts[:, :, :], wts[:, :, :], small[:, 32:48].unsqueeze(2).broadcast_to([P, NT, E]),
                                         ALU.mult))
            dve.wait_ge(rank_ps, 1)
            cnt = small[:, 64:128]
            link(nc.vector.tensor_scalar(cnt, ps[:, 2, 0:E], float(P - 1), None, ALU.add))
            ci = small[:, 128:192].bitcast(I32)
            cj = small[:, 192:256].bitcast(I32)
            link(nc.vector.tensor_copy(ci, cnt))
            link(nc.vector.tensor_scalar(cj, ci, 7, None, ALU.arith_shift_right))
            nt = small[:, 256:320]
            link(nc.vector.tensor_copy(nt, cj))
            ends = small[:, 320:384]
            link(nc.vector.tensor_tensor_scan(ends, nt, nt, 0.0, ALU.add, ALU.bypass))
            first = small[:, 384:448]
            link(nc.vector.tensor_tensor(first, ends, nt, ALU.subtract))
            link(nc.vector.tensor_scalar(first, first, float(P), 1.0, ALU.mult, ALU.add))
            link(nc.vector.tensor_tensor(small[0:E, 448:512], ends[0:E, :], ident[0:E, 0:E], ALU.mult))
            link(nc.vector.tensor_reduce(small[0:E, 512:513], small[0:E, 448:512], AX, ALU.add))
            nc.vector.tensor_scalar(tcmp_b[0:E, 0:NT_FFN], iota_t[:, 0:NT_FFN], small[0:E, 512:513], None,
                                    ALU.is_ge).then_inc(tcol_ok, 1)
            for k in range(2):
                s = slot[:, 8 * k:8 * k + 8, :]
                link(nc.vector.tensor_tensor(s, ps[:, k, :].rearrange("p (t e) -> p t e", e=E),
                                             first.unsqueeze(1).broadcast_to([P, 8, E]), ALU.add))
            link(nc.vector.tensor_tensor(slot[:, :, :], slot[:, :, :], chosen[:, :, :], ALU.mult))
            for t in range(NT):
                ins = nc.vector.max(stop8[:, t, :], slot[:, t, :])
            link(ins)
            nc.vector.tensor_scalar(slot_i[:, :, :], stop8[:, :, :], -1.0, None, ALU.add)
            for k in range(TOPK):
                link(nc.vector.tensor_tensor(tmp[:, :, :], slot[:, :, :], stop8[:, :, k:k + 1].broadcast_to([P, NT, E]),
                                             ALU.is_equal))
                link(nc.vector.tensor_tensor(tmp[:, :, :], tmp[:, :, :], wts[:, :, :], ALU.mult))
                link(nc.vector.tensor_reduce(w_top[:, :, k:k + 1], tmp[:, :, :], AX, ALU.add))
            dve.wait_ge(te_ps, 1)
            nc.vector.tensor_scalar(tile_e[:, :], ps[0:1, 3, 0:NT_FFN], float(E - 1), None, ALU.min).then_inc(route_ok, 1)

            for u in range(2):
                ins = nc.vector.memset(k_st[u][SROWS:XROWS, :, :], -1.0)
            ins.then_inc(minus_ok, 1)
            steps = [0]

            def drain_max(k, fill, slot_):
                c, t, h, kc, w = MAXU[k]
                dve.wait_ge(mx_full, fill + 1)
                nc.vector.tensor_reduce(mx[c][kc][:, t % 4, h:h + 1], MX[slot_ % MX_RING][:, 0:w], AX,
                                        ALU.max).then_inc(mx_done, 1)

            def split_max(c, done, base_):
                dve.wait_ge(mx_done, done)
                mo = m_parts[c]
                if c == 0:
                    nc.vector.tensor_copy(m_all[:, :, :], mx[0][0][:, :, :]).then_inc(m_step, 1)
                else:
                    nc.vector.tensor_tensor(m_all[:, :, :], mx[1][0][:, :, :], mx[1][1][:, :, :], ALU.max).then_inc(m_step, 1)
                dve.wait_ge(m_step, base_ + 1)
                nc.vector.tensor_copy(mo[:, :, :, 0], m_all[:, :, :]).then_inc(m_step, 1)
                dve.wait_ge(m_step, base_ + 2)
                nc.vector.tensor_tensor(m_res[:, :, :], m_all[:, :, :], mo[:, :, :, 0], ALU.subtract).then_inc(m_step, 1)
                dve.wait_ge(m_step, base_ + 3)
                nc.vector.tensor_copy(mo[:, :, :, 1], m_res[:, :, :]).then_inc(m_step, 1)
                dve.wait_ge(m_step, base_ + 4)
                nc.vector.tensor_tensor(mo[:, :, :, 2], m_res[:, :, :], mo[:, :, :, 1], ALU.subtract).then_inc(m_ok, 1)

            def row(c, slot_, fill, g):
                dve.wait_ge(mx_full, fill + 1)
                dve.wait_ge(mrow_in[c], g * ROW_INC + 16)
                nc.vector.tensor_copy(m_row[c][0:12, :], MX[slot_ % MX_RING].bitcast(BF16)[0:12, 0:CH])\
                    .then_inc(mx_done, 1)

            def group(g, u, last=False):
                fill = g * MX_BODY + MX_HEAD
                slot_ = MX_HEAD + MX_BODY * u
                row(1, slot_, fill, g)
                fill, slot_ = fill + 1, slot_ + 1
                if last:
                    return
                for k in range(N_MAX):
                    if k == MROW0_AFTER:
                        row(0, slot_, fill, g + 1)
                        fill, slot_ = fill + 1, slot_ + 1
                    drain_max(k, fill, slot_)
                    fill, slot_ = fill + 1, slot_ + 1
                    if k == N_MAX0 - 1:
                        split_max(0, fill, (g + 1) * 8)
                split_max(1, fill, (g + 1) * 8 + 4)

            fill = 0
            for k in range(N_MAX):
                drain_max(k, fill, fill)
                fill += 1
                if k == N_MAX0 - 1:
                    split_max(0, fill, 0)
            row(0, fill, fill, 0)
            fill += 1
            split_max(1, fill, 4)
            with dve.Fori(0, NG // 2 - 1) as i:
                for u in range(2):
                    group(i * 2 + u, u)

            def slot_work(s, k):
                static = isinstance(s, int)
                if not static or 1 <= s < NT_FFN + 1:
                    t, kt = s - 1, k - 1
                    gu = ps[:, 2 + kt % 2, :]
                    dve.wait_ge(th_ok, t + 1)
                    if not static or t >= 2:
                        dve.wait_ge(z_ok, t - 1)
                    nc.vector.scalar_tensor_tensor(out=fa[kt % 2], in0=fth[kt % 2][:, :], scalar=1.0, in1=gu[:, 0:INTER],
                                                   op0=ALU.add, op1=ALU.mult).then_inc(fa_ok, 1)
                    dve.wait_ge(fa_ok, t + 1)
                    if not static or t >= 2:
                        dve.wait_ge(zt_ps, t - 1)
                    nc.vector.tensor_tensor(fz[kt % 2][:, :], fa[kt % 2], gu[:, INTER:GU], ALU.mult).then_inc(z_ok, 1)
                if not static or 2 <= s < NT_FFN + 2:
                    t, kt = s - 2, k - 2
                    dve.wait_ge(zt_ps, t + 1)
                    if not static or t >= 2:
                        dve.wait_ge(y_ps, t - 1)
                    nc.vector.tensor_copy(fzT[kt % 2][:, :], ps[0:INTER, 4 + kt % 2, 0:P]).then_inc(zt_ok, 1)

            for s in range(RING):
                slot_work(s, s)
            with dve.Fori(1, NT_FFN // RING) as i:
                for r in range(RING):
                    slot_work(i * RING + r, r + RING)
            for s in range(NT_FFN, NT_FFN + 2):
                slot_work(s, s)

            group(NG - 2, 0)
            group(NG - 1, 1, last=True)

            n = 0
            for g in range(NG):
                for c in range(2):
                    dve.wait_ge(den_ps, n + 1)
                    nc.vector.reciprocal(rec[n % 2], ps[:, n % 2, :]).then_inc(rec_ok, 1)
                    dve.wait_ge(rec_ok, n + 1)
                    ov = o_sb[:, g, c * CH:(c + 1) * CH]
                    nc.vector.tensor_tensor(ov, ov, rec[n % 2], ALU.mult).then_inc(o_ok, 1)
                    n += 1
                if g % 4 == 3:
                    for t in range(8):
                        m = 8 * (g // 4) + t
                        dve.wait_ge(pr_ps, m + 1)
                        nc.vector.tensor_tensor(xs[:, m, :], ps[:, 2 + m % 2, 0:D], xs[:, m, :], ALU.add).then_inc(attn_ok, 1)
            for n in range(NT * TOPK):
                t, k = divmod(n, TOPK)
                dve.wait_ge(yg_in[n % YG], 16 * (n // YG + 1))
                dve.wait_ge(attn_ok, t + 1) if k == 0 else dve.wait_ge(moe_step, n)
                nc.vector.scalar_tensor_tensor(out=xs[:, t, :], in0=yg[n % YG], scalar=w_top[:, t, k:k + 1],
                                               in1=xs[:, t, :], op0=ALU.mult, op1=ALU.add).then_inc(moe_step, 1)


def kernel(L0_attn_x, L0_attn_lora_start_indices, L0_attn_Wq, L0_attn_Aq, L0_attn_Bq, L0_attn_Wk, L0_attn_Ak,
           L0_attn_Bk, L0_attn_Wv, L0_attn_Av, L0_attn_Bv, L0_attn_Wo, L0_attn_Ao, L0_attn_Bo, L0_ffn_gate_w,
           L0_ffn_Wg, L0_ffn_Wu, L0_ffn_Wd):
    import concourse.bacc as bacc
    from concourse.bass_utils import run_bass_kernel_spmd

    f = np.float32
    a = lambda v: np.asarray(v)
    order = np.arange(D).reshape(H, HALF, 2).transpose(2, 0, 1).reshape(-1)
    rows = lambda w: w.T.reshape(DC, P, -1).transpose(1, 0, 2)
    w_qkv = np.stack([rows(a(L0_attn_Wq)[order]), rows(a(L0_attn_Wk)[order]), rows(a(L0_attn_Wv))], 1)
    w_o = np.zeros((H // HG, HG, 32, D), f)
    w_o[:, :, :DK] = a(L0_attn_Wo).T.reshape(H // HG, HG, DK, D)
    w_o = w_o.reshape(H // HG, P, D).transpose(1, 0, 2)
    flat = lambda v: a(v).reshape(N_LORA * RANK, D)
    lora_a = np.stack([flat(L0_attn_Aq), flat(L0_attn_Ak), flat(L0_attn_Av)], 1)
    lora_ao = np.zeros((N_LORA * RANK, H // HG, HG, 32), f)
    lora_ao[..., :DK] = flat(L0_attn_Ao).reshape(-1, H // HG, HG, DK)
    lora_ao = lora_ao.reshape(N_LORA * RANK, H // HG, P)
    down = lambda v: a(v).transpose(0, 2, 1).reshape(N_LORA * RANK, D)
    lora_b = np.stack([down(L0_attn_Bq)[:, order], down(L0_attn_Bk)[:, order], down(L0_attn_Bv), down(L0_attn_Bo)], 1)
    gate = rows(a(L0_ffn_gate_w))
    w_gu = np.concatenate([a(L0_ffn_Wg), a(L0_ffn_Wu)], 1).transpose(0, 2, 1)
    w_gu = w_gu.reshape(E, DC, P, GU).transpose(0, 2, 1, 3).reshape(E, P, DC * GU)
    w_d = a(L0_ffn_Wd).transpose(0, 2, 1)

    inv = (f(10000.0) ** (-np.arange(0, DK, 2, dtype=f) / f(DK))).astype(f)
    ang = (np.arange(SEQ, dtype=f)[None, :] * inv[:, None]).astype(f)
    cos, sin = np.tile(np.cos(ang), (H, 1)), np.tile(np.sin(ang), (H, 1))
    i = np.arange(P)
    consts = np.zeros((P, 8, P), f)
    consts[:, 0] = np.eye(P)
    consts[:, 1] = np.where(i[None, :] <= i[:, None], 0, NEG)
    consts[:, 2] = np.where(i[:, None] <= i[None, :], 0, NEG)
    consts[:, 3] = i[:, None] == 32 * (i[None, :] // 32) + DK
    consts[:, 4] = i[:, None] < i[None, :]
    consts[:, 5] = 1
    rowc = np.zeros((E, NT_FFN + 2), f)
    rowc[:, :NT_FFN] = np.arange(NT_FFN)
    rowc[:, NT_FFN] = np.arange(E) // RANK

    arrays = dict(x=a(L0_attn_x).reshape(TOK, D), lora=a(L0_attn_lora_start_indices), w_qkv=w_qkv, w_o=w_o,
                  lora_a=lora_a, lora_ao=lora_ao, lora_b=lora_b, gate=gate, w_gu=w_gu, w_d=w_d, cos=cos, sin=sin,
                  consts=consts, rowc=rowc)
    arrays = {k: np.ascontiguousarray(v) for k, v in arrays.items()}
    nc = bacc.Bacc("TRN2", target_bir_lowering=False, num_devices=1)
    args = {k: nc.dram_tensor(k, v.shape, mybir.dt.from_np(v.dtype), kind="ExternalInput").ap()
            for k, v in arrays.items()}
    out = nc.dram_tensor("out", (TOK, D), F32, kind="ExternalOutput").ap()
    build(nc, out=out, **args)
    r = run_bass_kernel_spmd(nc, [arrays], core_ids=[0])
    return r.results[0]["out"].reshape(BATCH, SEQ, D)
```
